# Optimizing a Trainium2 kernel written in Bass

```python
import numpy as np
import jax
import jax.numpy as jnp

def _softmax(x, axis=-1):
    return jax.nn.softmax(x, axis=axis)

def _gelu(x):
    return jax.nn.gelu(x, approximate=True)

def _silu(x):
    return jax.nn.silu(x)

def _sigmoid(x):
    return jax.nn.sigmoid(x)

def _layernorm(x, axis=-1, eps=1e-05):
    m = jnp.mean(x, axis=axis, keepdims=True)
    v = jnp.var(x, axis=axis, keepdims=True)
    return (x - m) / jnp.sqrt(v + eps)

def _scatter_add(tgt, idx, src, axis=0):
    return tgt.at[idx].add(src)

def _segment_sum(src, seg, n):
    return jax.ops.segment_sum(src, seg, n)
kernel_name = 'mk_macaron_d2_jaxref_r8_5f0de3'

def setup_inputs(seed: int=0):
    np.random.seed(seed)
    _w = jnp.asarray

    def _L0_attn_setup():
        import jax, jax.numpy as jnp
        import numpy as np
        DIM = 128
        HEADS = 16
        DIM_HEAD = 64
        DIM_INNER = HEADS * DIM_HEAD
        SCALE = DIM_HEAD ** (-0.5)

        def rmsnorm(x, w):
            eps = jnp.asarray(jnp.finfo(x.dtype).eps, x.dtype)
            var = jnp.mean(jnp.square(x), axis=-1, keepdims=True)
            return x * jax.lax.rsqrt(var + eps) * w
        key = jax.random.key(seed)
        ks = jax.random.split(key, 6)
        tokens = jax.random.normal(ks[0], (2, 256, DIM), dtype=jnp.float32)
        norm_w = jnp.ones((DIM,), dtype=jnp.float32)
        Wq = jax.random.normal(ks[1], (DIM, DIM_INNER), dtype=jnp.float32) * 0.02
        Wkv = jax.random.normal(ks[2], (DIM, 2 * DIM_INNER), dtype=jnp.float32) * 0.02
        Wout = jax.random.normal(ks[3], (DIM_INNER, DIM), dtype=jnp.float32) * 0.02
        Wg = jax.random.normal(ks[4], (DIM, HEADS), dtype=jnp.float32) * 0.02
        return {'tokens': tokens, 'norm_w': norm_w, 'Wq': Wq, 'Wkv': Wkv, 'Wout': Wout, 'Wg': Wg}
    _L0_attn_in = _L0_attn_setup()

    def _L0_ffn_setup():
        import jax, jax.numpy as jnp
        import numpy as np
        EPS = 1e-05

        def _quantize(W):
            gamma = jnp.mean(jnp.abs(W))
            return jnp.clip(jnp.round(W / (gamma + EPS)), -1.0, 1.0)
        key = jax.random.key(seed)
        k_x, k_w1, k_b1, k_w2, k_b2 = jax.random.split(key, 5)
        n_embd = 128
        d_ff = 4 * n_embd
        B, S = (4, 512)
        bound1 = 1.0 / np.sqrt(n_embd)
        bound2 = 1.0 / np.sqrt(d_ff)
        x = jax.random.normal(k_x, (B, S, n_embd), dtype=jnp.float32)
        W1 = jax.random.uniform(k_w1, (d_ff, n_embd), jnp.float32, -bound1, bound1)
        b1 = jax.random.uniform(k_b1, (d_ff,), jnp.float32, -bound1, bound1)
        W2 = jax.random.uniform(k_w2, (n_embd, d_ff), jnp.float32, -bound2, bound2)
        b2 = jax.random.uniform(k_b2, (n_embd,), jnp.float32, -bound2, bound2)
        return {'x': x, 'W1': W1, 'b1': b1, 'W2': W2, 'b2': b2}
    _L0_ffn_in = _L0_ffn_setup()

    def _L1_attn_setup():
        import jax, jax.numpy as jnp
        import numpy as np
        DIM = 128
        HEADS = 16
        DIM_HEAD = 64
        INNER = HEADS * DIM_HEAD

        def _attention(x, ln_gamma, ln_beta, w_qkv, w_out, b_out):
            b, n, _ = x.shape
            scale = DIM_HEAD ** (-0.5)
            mu = jnp.mean(x, axis=-1, keepdims=True)
            var = jnp.var(x, axis=-1, keepdims=True)
            xn = (x - mu) / jnp.sqrt(var + 1e-05) * ln_gamma + ln_beta
            qkv = jnp.einsum('bnd,ed->bne', xn, w_qkv)
            q, k, v = jnp.split(qkv, 3, axis=-1)
            reshape = lambda t: t.reshape(b, n, HEADS, DIM_HEAD).transpose(0, 2, 1, 3)
            q, k, v = (reshape(q) * scale, reshape(k), reshape(v))
            sim = jnp.einsum('bhid,bhjd->bhij', q, k)
            mask_value = -jnp.finfo(sim.dtype).max
            causal = jnp.triu(jnp.ones((n, n), dtype=bool), k=1)
            sim = jnp.where(causal, mask_value, sim)
            sim = sim - jax.lax.stop_gradient(jnp.max(sim, axis=-1, keepdims=True))
            attn = jax.nn.softmax(sim, axis=-1)
            out = jnp.einsum('bhij,bhjd->bhid', attn, v)
            out = out.transpose(0, 2, 1, 3).reshape(b, n, INNER)
            return jnp.einsum('bne,de->bnd', out, w_out) + b_out
        key = jax.random.key(seed)
        ks = jax.random.split(key, 6)
        x = jax.random.normal(ks[0], (2, 256, DIM), dtype=jnp.float32)
        ln_gamma = jnp.ones((DIM,), dtype=jnp.float32)
        ln_beta = jnp.zeros((DIM,), dtype=jnp.float32)
        w_qkv = jax.random.normal(ks[1], (3 * INNER, DIM), dtype=jnp.float32) * DIM ** (-0.5)
        w_out = jax.random.normal(ks[2], (DIM, INNER), dtype=jnp.float32) * INNER ** (-0.5)
        b_out = jax.random.normal(ks[3], (DIM,), dtype=jnp.float32) * 0.02
        return {'x': x, 'ln_gamma': ln_gamma, 'ln_beta': ln_beta, 'w_qkv': w_qkv, 'w_out': w_out, 'b_out': b_out}
    _L1_attn_in = _L1_attn_setup()

    def _L1_ffn_setup():
        import jax, jax.numpy as jnp
        import numpy as np
        B, T, D = (1, 128, 128)
        E, S, H = (8, 2, 512)
        key = jax.random.key(seed)
        kx, kg, k1, k2, k3 = jax.random.split(key, 5)
        X = jax.random.normal(kx, (B, T, D), jnp.float32)
        Wg = jax.random.normal(kg, (D, E), jnp.float32) * 0.02
        bg = jnp.zeros((E,), jnp.float32)
        W1 = jax.random.normal(k1, (E, D, H), jnp.float32) * 0.02
        W3 = jax.random.normal(k3, (E, D, H), jnp.float32) * 0.02
        W2 = jax.random.normal(k2, (E, H, D), jnp.float32) * 0.02
        return {'X': X, 'Wg': Wg, 'bg': bg, 'W1': W1, 'W2': W2, 'W3': W3}
    _L1_ffn_in = _L1_ffn_setup()
    _d = {'L0_attn_tokens': _L0_attn_in['tokens'], 'L0_attn_norm_w': _L0_attn_in['norm_w'], 'L0_attn_Wq': _L0_attn_in['Wq'], 'L0_attn_Wkv': _L0_attn_in['Wkv'], 'L0_attn_Wout': _L0_attn_in['Wout'], 'L0_attn_Wg': _L0_attn_in['Wg'], 'L0_ffn_W1': _L0_ffn_in['W1'], 'L0_ffn_b1': _L0_ffn_in['b1'], 'L0_ffn_W2': _L0_ffn_in['W2'], 'L0_ffn_b2': _L0_ffn_in['b2'], 'L1_attn_ln_gamma': _L1_attn_in['ln_gamma'], 'L1_attn_ln_beta': _L1_attn_in['ln_beta'], 'L1_attn_w_qkv': _L1_attn_in['w_qkv'], 'L1_attn_w_out': _L1_attn_in['w_out'], 'L1_attn_b_out': _L1_attn_in['b_out'], 'L1_ffn_Wg': _L1_ffn_in['Wg'], 'L1_ffn_bg': _L1_ffn_in['bg'], 'L1_ffn_W1': _L1_ffn_in['W1'], 'L1_ffn_W2': _L1_ffn_in['W2'], 'L1_ffn_W3': _L1_ffn_in['W3']}
    _x0 = _d['L0_attn_tokens']
    _d['L0_attn_tokens'] = jax.random.normal(jax.random.fold_in(jax.random.key(seed), 1), (4, 512, 128), dtype=_x0.dtype)
    del _x0
    return _d

def reference(L0_attn_tokens, L0_attn_norm_w, L0_attn_Wq, L0_attn_Wkv, L0_attn_Wout, L0_attn_Wg, L0_ffn_W1, L0_ffn_b1, L0_ffn_W2, L0_ffn_b2, L1_attn_ln_gamma, L1_attn_ln_beta, L1_attn_w_qkv, L1_attn_w_out, L1_attn_b_out, L1_ffn_Wg, L1_ffn_bg, L1_ffn_W1, L1_ffn_W2, L1_ffn_W3):

    def _L0_attn_ref(tokens, norm_w, Wq, Wkv, Wout, Wg):
        import jax, jax.numpy as jnp
        import numpy as np
        DIM = 128
        HEADS = 16
        DIM_HEAD = 64
        DIM_INNER = HEADS * DIM_HEAD
        SCALE = DIM_HEAD ** (-0.5)

        def rmsnorm(x, w):
            eps = jnp.asarray(jnp.finfo(x.dtype).eps, x.dtype)
            var = jnp.mean(jnp.square(x), axis=-1, keepdims=True)
            return x * jax.lax.rsqrt(var + eps) * w
        b, n, _ = tokens.shape
        x = rmsnorm(tokens, norm_w)
        q = x @ Wq
        kv = x @ Wkv
        k, v = jnp.split(kv, 2, axis=-1)

        def split_heads(t):
            return t.reshape(b, n, HEADS, DIM_HEAD).transpose(0, 2, 1, 3)
        q, k, v = map(split_heads, (q, k, v))
        sim = jnp.einsum('bhid,bhjd->bhij', q, k) * SCALE
        causal_mask = jnp.triu(jnp.ones((n, n), dtype=bool), k=1)
        sim = jnp.where(causal_mask, jnp.asarray(-jnp.finfo(sim.dtype).max, sim.dtype), sim)
        attn = jax.nn.softmax(sim, axis=-1)
        out = jnp.einsum('bhij,bhjd->bhid', attn, v)
        gates = jax.nn.sigmoid(x @ Wg)
        gates = gates.transpose(0, 2, 1)[..., None]
        out = gates * out
        out = out.transpose(0, 2, 1, 3).reshape(b, n, DIM_INNER)
        return out @ Wout

    def _L0_ffn_ref(x, W1, b1, W2, b2):
        import jax, jax.numpy as jnp
        import numpy as np
        EPS = 1e-05

        def _quantize(W):
            gamma = jnp.mean(jnp.abs(W))
            return jnp.clip(jnp.round(W / (gamma + EPS)), -1.0, 1.0)
        Wq1 = _quantize(W1)
        Wq2 = _quantize(W2)
        h = jax.nn.relu(jnp.einsum('bsd,fd->bsf', x, Wq1) + b1)
        out = jnp.einsum('bsf,df->bsd', h, Wq2) + b2
        return out

    def _L1_attn_ref(x, ln_gamma, ln_beta, w_qkv, w_out, b_out):
        import jax, jax.numpy as jnp
        import numpy as np
        DIM = 128
        HEADS = 16
        DIM_HEAD = 64
        INNER = HEADS * DIM_HEAD

        def _attention(x, ln_gamma, ln_beta, w_qkv, w_out, b_out):
            b, n, _ = x.shape
            scale = DIM_HEAD ** (-0.5)
            mu = jnp.mean(x, axis=-1, keepdims=True)
            var = jnp.var(x, axis=-1, keepdims=True)
            xn = (x - mu) / jnp.sqrt(var + 1e-05) * ln_gamma + ln_beta
            qkv = jnp.einsum('bnd,ed->bne', xn, w_qkv)
            q, k, v = jnp.split(qkv, 3, axis=-1)
            reshape = lambda t: t.reshape(b, n, HEADS, DIM_HEAD).transpose(0, 2, 1, 3)
            q, k, v = (reshape(q) * scale, reshape(k), reshape(v))
            sim = jnp.einsum('bhid,bhjd->bhij', q, k)
            mask_value = -jnp.finfo(sim.dtype).max
            causal = jnp.triu(jnp.ones((n, n), dtype=bool), k=1)
            sim = jnp.where(causal, mask_value, sim)
            sim = sim - jax.lax.stop_gradient(jnp.max(sim, axis=-1, keepdims=True))
            attn = jax.nn.softmax(sim, axis=-1)
            out = jnp.einsum('bhij,bhjd->bhid', attn, v)
            out = out.transpose(0, 2, 1, 3).reshape(b, n, INNER)
            return jnp.einsum('bne,de->bnd', out, w_out) + b_out
        return _attention(x, ln_gamma, ln_beta, w_qkv, w_out, b_out)

    def _L1_ffn_ref(X, Wg, bg, W1, W2, W3):
        import jax, jax.numpy as jnp
        import numpy as np
        B, T, D = (1, 128, 128)
        E, S, H = (8, 2, 512)
        logits = jnp.einsum('btd,de->bte', X, Wg) + bg
        topv, topi = jax.lax.top_k(logits, S)
        w = jax.nn.softmax(topv, axis=-1)
        xs = X[:, :, None, :] * w[..., None]
        out = X
        for e in range(E):
            h = jax.nn.silu(jnp.einsum('btsd,dh->btsh', xs, W1[e])) * jnp.einsum('btsd,dh->btsh', xs, W3[e])
            y = jnp.einsum('btsh,hd->btsd', h, W2[e])
            mask = (topi == e)[..., None]
            out = out + jnp.where(mask, y, 0.0).sum(axis=2)
        return out
    x = L0_attn_tokens
    x = x + 0.5 * _L0_ffn_ref(_layernorm(x, axis=-1), L0_ffn_W1, L0_ffn_b1, L0_ffn_W2, L0_ffn_b2)
    x = x + _L0_attn_ref(_layernorm(x, axis=-1), L0_attn_norm_w, L0_attn_Wq, L0_attn_Wkv, L0_attn_Wout, L0_attn_Wg)
    x = x + 0.5 * _L0_ffn_ref(_layernorm(x, axis=-1), L0_ffn_W1, L0_ffn_b1, L0_ffn_W2, L0_ffn_b2)
    x = x + 0.5 * _L1_ffn_ref(_layernorm(x, axis=-1), L1_ffn_Wg, L1_ffn_bg, L1_ffn_W1, L1_ffn_W2, L1_ffn_W3)
    x = x + _L1_attn_ref(_layernorm(x, axis=-1), L1_attn_ln_gamma, L1_attn_ln_beta, L1_attn_w_qkv, L1_attn_w_out, L1_attn_b_out)
    x = x + 0.5 * _L1_ffn_ref(_layernorm(x, axis=-1), L1_ffn_Wg, L1_ffn_bg, L1_ffn_W1, L1_ffn_W2, L1_ffn_W3)
    return x

_drawn_inputs = setup_inputs


def setup_inputs(seed=0):
    import zlib

    import numpy as np

    out = dict(_drawn_inputs(seed))
    spreads = {'L0_attn_norm_w': (1.0, 0.6),
     'L1_attn_ln_gamma': (1.0, 0.6),
     'L1_attn_ln_beta': (0.0, 0.8),
     'L1_ffn_bg': (0.0, 2.0)}
    factors = {'L0_attn_Wq': 8.0,
     'L0_attn_Wkv': 8.0,
     'L0_attn_Wout': 8.0,
     'L0_attn_Wg': 8.0,
     'L0_ffn_b1': 8.0,
     'L0_ffn_b2': 64.0,
     'L1_attn_w_qkv': 8.0,
     'L1_attn_w_out': 8.0,
     'L1_attn_b_out': 200.0,
     'L1_ffn_Wg': 8.0,
     'L1_ffn_W1': 8.0,
     'L1_ffn_W2': 8.0,
     'L1_ffn_W3': 8.0}
    for name, (base, spread) in spreads.items():
        noise = np.random.default_rng([zlib.crc32(name.encode()), seed]).standard_normal(out[name].shape)
        drawn = base * np.exp(spread * noise) if base else spread * noise
        out[name] = jnp.asarray(drawn.astype(out[name].dtype))
    for name, factor in factors.items():
        out[name] = (out[name] * factor).astype(out[name].dtype)
    return out
```

```python
import math
from contextlib import ExitStack

import concourse.bass as bass
from concourse import mybir
from concourse.bass import ds

F32 = mybir.dt.float32
F16 = mybir.dt.float16
BF16 = mybir.dt.bfloat16
I32 = mybir.dt.int32
U32 = mybir.dt.uint32
ALU = mybir.AluOpType
ACT = mybir.ActivationFunctionType
AX = mybir.AxisListType

PHASES = ("ffn", "attn0", "ffn", "moe", "attn1", "moe")


def macaron_block(nc: bass.Bass, ins, out, phases):
    tokens = ins["L0_attn_tokens"]
    NB, SEQ, D = tokens.shape
    P = 128
    TOK = NB * SEQ
    NT = TOK // P
    TPB = SEQ // P
    CH = 512
    NCH = TOK // CH
    TPC = CH // P
    INNER = ins["L0_attn_Wq"].shape[1]
    HEADS = ins["L0_attn_Wg"].shape[1]
    DH = INNER // HEADS
    PAIRS = HEADS // 2
    ITEMS = NB * PAIRS
    DFF = ins["L0_ffn_W1"].shape[0]
    FB = DFF // P
    EXPERTS, _, H = ins["L1_ffn_W1"].shape
    HB = H // P
    TOPK = 2
    ETILES = (TOPK * TOK + EXPERTS * (P - 1)) // P
    W_UP = 64.0
    LN_EPS = 1e-5
    RMS_EPS = 2.0 ** -23
    Q_SCALE = DH ** -0.5 / W_UP
    EXP_LIFT = 4.0
    NEG = -1e30
    assert (P, CH, 2 * DH, TPC, TPB, HB) == (128, 512, 128, 4, 4, 4) and D == P

    ctx = ExitStack()
    with ctx:
        def sb(name, shape, dt):
            return ctx.enter_context(nc.sbuf_tensor(name, shape, dt))

        def sem(name):
            return ctx.enter_context(nc.semaphore(name))

        X = sb("X", [P, NT, D], F32)
        XN = sb("XN", [P, NT, D], F32)
        XTh = sb("XTh", [P, TOK], F16)
        XTl = sb("XTl", [P, TOK], F16)
        T32 = sb("T32", [P, CH], F32)
        ident = sb("ident", [P, P], F32)
        identh = sb("identh", [P, P], F16)
        identb = sb("identb", [P, P], BF16)
        mask_qk = sb("mask_qk", [P, P], BF16)
        mask_kq = sb("mask_kq", [P, P], BF16)
        ones32 = sb("ones32", [P, P], F32)
        onesh = sb("onesh", [P, P], F16)
        before = sb("before", [P, P], F16)
        neghalf = sb("neghalf", [P, NT], F32)
        bst = sb("bst", [P, NT, 6], F32)
        mv = sb("mv", [P, NT, 2], F32)
        rstd = sb("rstd", [P, NT], F32)
        pw = sb("pw", [P, 4, NT], F32)
        b1c = sb("b1c", [P, FB], F32)
        b2h = sb("b2h", [P, D], F32)
        bout = sb("bout", [P, D], F32)
        normw = sb("normw", [P, 1], F32)
        gamma = sb("gamma", [P, 1], F32)
        beta = sb("beta", [P, 1], F32)
        bgate = sb("bgate", [P, EXPERTS], F32)
        F1 = sb("F1", [P, FB, P], F16)
        F2 = sb("F2", [P, FB, D], F16)
        fsm = sb("fsm", [P, 2, 4], F32)
        WQh = sb("WQh", [P, HEADS, 2, DH], F16)
        WQl = sb("WQl", [P, HEADS, 2, DH], F16)
        WKh = sb("WKh", [P, HEADS, 2, DH], F16)
        WKl = sb("WKl", [P, HEADS, 2, DH], F16)
        WVh = sb("WVh", [P, INNER], F16)
        WVl = sb("WVl", [P, INNER], F16)
        WOh = sb("WOh", [P, PAIRS, D], F16)
        WOl = sb("WOl", [P, PAIRS, D], F16)
        WGh = sb("WGh", [P, HEADS], F16)
        WGl = sb("WGl", [P, HEADS], F16)
        gates = sb("gates", [P, NT, HEADS], F32)
        E1h = sb("E1h", [P, EXPERTS, H], F16)
        E1l = sb("E1l", [P, EXPERTS, H], F16)
        E3h = sb("E3h", [P, EXPERTS, H], F16)
        E3l = sb("E3l", [P, EXPERTS, H], F16)
        E2h = sb("E2h", [P, EXPERTS, HB, D], F16)
        E2l = sb("E2l", [P, EXPERTS, HB, D], F16)
        RGh = sb("RGh", [P, EXPERTS], F16)
        RGl = sb("RGl", [P, EXPERTS], F16)
        small = sb("small", [P, 32], F32)
        iota_e = sb("iota_e", [P, NT, EXPERTS], F32)
        iota_t = sb("iota_t", [P, ETILES, EXPERTS], F32)
        upto = sb("upto", [P, EXPERTS, EXPERTS], F32)

        stage = sb("stage", [P, 2, 4 * H], F32)

        ARENA = 19712
        arena = sb("arena", [P, ARENA], F32)
        used = [0]

        def carve(shape, dt):
            size = math.prod(shape)
            words = size if dt in (F32, I32, U32) else size // 2
            at = used[0]
            used[0] += words
            assert used[0] <= ARENA, used[0]
            v = arena[:, at:at + words]
            if dt != F32:
                v = v.bitcast(dt)
            names = "abcdef"[:len(shape)]
            if len(shape) > 1:
                v = v.rearrange(f"p ({' '.join(names)}) -> p {' '.join(names)}",
                                **{c: s for c, s in zip(names, shape)})
            return v

        h32 = carve([2, CH], F32)
        HH = carve([2, FB, CH], F16)
        HL = carve([2, FB, CH], F16)
        used[0] = 0
        RING = 4
        Q1 = carve([RING, 2, CH], F16)
        Q2 = carve([RING, 2, CH], F16)
        K1 = carve([RING, 2, CH], F16)
        K2 = carve([RING, 2, CH], F16)
        VH = carve([RING, TPB, 2, DH + 2], F16)
        VL = carve([RING, TPB, 2, DH], F16)
        P32 = carve([5, CH], F32)
        PH = carve([2, 5, CH], F16)
        PL = carve([2, 5, CH], F16)
        O32 = carve([TPB, 2, DH], F32)
        OH = carve([TPB, 2 * DH], F16)
        OL = carve([TPB, 2 * DH], F16)
        OTh = carve([CH], F16)
        OTl = carve([CH], F16)
        MX = carve([2, TPB], F32)
        osc = carve([2, 2, TPB], F32)
        used[0] = 0
        XSs = carve([NT, TOPK, 2, D], F16)
        XSt = carve([ETILES, 2 * D], F16)
        Gy = XSs.rearrange("p a b c d -> p (a b c d)").bitcast(F32)
        used[0] = NT * TOPK * D + ETILES * D
        logits = carve([NT, EXPERTS], F32)
        top8 = carve([NT, 8], F32)
        idx8 = carve([NT, 8], U32)
        idxf = carve([TOPK, NT], F32)
        hot = carve([TOPK, NT, EXPERTS], F32)
        hoth = carve([NT, EXPERTS], F16)
        prod = carve([TOPK, NT, EXPERTS], F32)
        wts = carve([4, NT], F32)
        posf = carve([TOPK, NT], F32)
        posi = carve([TOPK, NT], I32)
        cnt_i = carve([2, EXPERTS], I32)
        cnt = carve([4, EXPERTS], F32)
        cum = carve([EXPERTS, EXPERTS], F32)
        tile_e8 = carve([ETILES, EXPERTS], F32)
        tile_e = carve([2, 64], F32)
        tile_ei = carve([64], I32)
        XTt = carve([2, 2, P], F16)
        SA = carve([2, H], F32)
        G32 = carve([2, H], F32)
        GH = carve([2, HB, P], F16)
        GL = carve([2, HB, P], F16)
        YS = carve([2, D], F32)

        ps = ctx.enter_context(nc.psum_tensor("ps", [P, 8, CH], F32))

        x_sorted = nc.dram_tensor("x_sorted", (ETILES * P, 2 * D), F16).ap()
        y_sorted = nc.dram_tensor("y_sorted", (ETILES * P, D), F32).ap()

        s_x_in = sem("x_in")
        s_small_in = sem("small_in")
        s_f_in = sem("f_in")
        s_zero_in = sem("zero_in")
        s_w_in = [sem("w_in0"), sem("w_in1")]
        s_out_done = sem("out_done")
        s_const_pool = sem("const_pool")
        s_dve_step = sem("dve_step")
        s_pool_step = sem("pool_step")
        s_f_abs = sem("f_abs")
        s_f_sum = sem("f_sum")
        s_f_tern = sem("f_tern")
        s_f_tp = sem("f_tp")
        s_f_got = sem("f_got")
        s_w_tp = sem("w_tp")
        s_w_hi = sem("w_hi")
        s_w_lo = sem("w_lo")
        s_ln_mv = sem("ln_mv")
        s_ln_rstd = sem("ln_rstd")
        s_ln_xn = sem("ln_xn")
        s_ln_tp = sem("ln_tp")
        s_ln_hi = sem("ln_hi")
        s_ln_lo = sem("ln_lo")
        s_up_ps = sem("up_ps")
        s_h_relu = sem("h_relu")
        s_h_hi = sem("h_hi")
        s_h_lo = sem("h_lo")
        s_dn_ps = sem("dn_ps")
        s_x_based = sem("x_based")
        s_x_att = sem("x_att")
        s_x_done = sem("x_done")
        s_g_ps = sem("g_ps")
        s_g_exp = sem("g_exp")
        s_qk_ps = sem("qk_ps")
        s_qk_hi = sem("qk_hi")
        s_qk_lo = sem("qk_lo")
        s_v_ps = sem("v_ps")
        s_v_hi = sem("v_hi")
        s_v_lo = sem("v_lo")
        s_k2_cp = sem("k2_cp")
        s_k2_set = sem("k2_set")
        s_mx_ps = sem("mx_ps")
        s_mx_red = sem("mx_red")
        s_mt_ps = sem("mt_ps")
        s_mt_sb = sem("mt_sb")
        s_st_ps = sem("st_ps")
        s_ex_p = sem("ex_p")
        s_ph = sem("ph")
        s_pl = sem("pl")
        s_av_ps = sem("av_ps")
        s_o_f = sem("o_f")
        s_o_ev = sem("o_ev")
        s_oh = sem("oh")
        s_ol = sem("ol")
        s_oth_ps = sem("oth_ps")
        s_otl_ps = sem("otl_ps")
        s_oth_sb = sem("oth_sb")
        s_otl_sb = sem("otl_sb")
        s_op_ps = sem("op_ps")
        s_r_ps = sem("r_ps")
        s_r_exp = sem("r_exp")
        s_r_hot = sem("r_hot")
        s_r_rank = sem("r_rank")
        s_r_pos = sem("r_pos")
        s_xs_rdy = sem("xs_rdy")
        s_xs_sent = sem("xs_sent")
        s_xs_in = sem("xs_in")
        s_t_ps = sem("t_ps")
        s_t_sb = sem("t_sb")
        s_ab_ps = sem("ab_ps")
        s_a_sb = sem("a_sb")
        s_g32_rdy = sem("g32_rdy")
        s_g_hi = sem("g_hi")
        s_g_lo = sem("g_lo")
        s_y_ps = sem("y_ps")
        s_y_sb = sem("y_sb")
        s_y_out = [sem("y_out0"), sem("y_out1")]
        s_y_got = [sem("y_got0"), sem("y_got1"), sem("y_got2"), sem("y_got3")]

        def stored(m, parity):
            return m * ((ETILES + 1 - parity) // 2)

        def stepper(eng, chain):
            n = [0]

            def step(ins):
                n[0] += 1
                ins.then_inc(chain, 1)
                eng.wait_ge(chain, n[0])
            return step

        plan = []
        seen = {"norm": 0, "ffn": 0, "attn": 0, "moe": 0}
        for ph in phases:
            plan.append((ph, dict(seen)))
            seen["norm"] += 1
            seen[ph.rstrip("01")] += 1
        has_attn1 = "attn1" in phases

        wq0 = ins["L0_attn_Wq"]
        wkv0 = ins["L0_attn_Wkv"]
        wout0 = ins["L0_attn_Wout"].rearrange("(c p) n -> p c n", p=P)
        wqkv1 = ins["L1_attn_w_qkv"].rearrange("(c p) d -> p c d", p=P)
        wout1 = ins["L1_attn_w_out"]

        def twice(v):
            return v.unsqueeze(2).broadcast_to([P, v.shape[1], 2, DH])

        pieces = []
        if "attn0" in phases:

            def heads(v, n):
                return v.rearrange("p (h d) -> p h d", h=n)
            pieces.append((wq0, INNER, lambda s: twice(heads(s, HEADS)), WQh[:], WQl[:]))
            pieces.append((wkv0[:, 0:INNER], INNER, lambda s: twice(heads(s, HEADS)), WKh[:], WKl[:]))
            pieces.append((wkv0[:, INNER:], INNER, lambda s: s, WVh[:], WVl[:]))
            pieces.append((wout0, INNER, lambda s: s.rearrange("p (c n) -> p c n", c=PAIRS), WOh[:], WOl[:]))
            pieces.append((ins["L0_attn_Wg"], HEADS, lambda s: s, WGh[:], WGl[:]))
        if "moe" in phases:
            for w, h, l in (("L1_ffn_W1", E1h, E1l), ("L1_ffn_W3", E3h, E3l)):
                for e in range(0, EXPERTS, 4):
                    pieces.append((ins[w][e:e + 4].rearrange("e p h -> p e h"), 4 * H,
                                   lambda s: s.rearrange("p (e h) -> p e h", e=4), h[:, e:e + 4, :], l[:, e:e + 4, :]))
            for e in range(0, EXPERTS, 4):
                pieces.append((ins["L1_ffn_W2"][e:e + 4].rearrange("e (c p) d -> p e c d", p=P), 4 * H,
                               lambda s: s.rearrange("p (e c d) -> p e c d", e=4, c=HB),
                               E2h[:, e:e + 4], E2l[:, e:e + 4]))
            pieces.append((ins["L1_ffn_Wg"], EXPERTS, lambda s: s, RGh[:], RGl[:]))
        NPIECE = len(pieces)

        def stage_as(i):
            src, cols = pieces[i][0], pieces[i][1]
            s = stage[:, i % 2, 0:cols]
            if len(src.shape) == 3:
                return s.rearrange("p (a b) -> p a b", a=src.shape[1])
            if len(src.shape) == 4:
                return s.rearrange("p (a b c) -> p a b c", a=src.shape[1], b=src.shape[2])
            return s

        LAGS = (0, 1, 2, 3, 4)

        def items(t):
            if not isinstance(t, int):
                return tuple(t - lag if lag else t for lag in LAGS)
            return tuple(t - lag if 0 <= t - lag < ITEMS else None for lag in LAGS)

        def seq_of(j):
            return j // PAIRS if isinstance(j, int) else (j >> int(math.log2(PAIRS))).with_bounds(min_val=0, max_val=NB - 1)

        def later(j, k):
            return not isinstance(j, int) or j >= k

        def run_items(eng, body):
            first = LAGS[-1] + 1
            for t in range(first):
                body(t)
            with eng.Fori(first, ITEMS) as t:
                body(t)
            for t in range(ITEMS, ITEMS + LAGS[-1]):
                body(t)

        MAX_UNITS = (((0, 3, 0),), ((0, 2, 0), (0, 0, 384)), ((1, 3, 0),), ((1, 2, 0), (1, 0, 384)),
                     ((0, 1, 0), (1, 1, 256)))
        EXP_UNITS = (((0, 0, 0),), ((0, 1, 0), (0, 3, 384)), ((1, 0, 0),), ((1, 1, 0), (1, 3, 384)),
                     ((0, 2, 0), (1, 2, 256)))
        WHERE = {(x, k): (u, at) for u, unit in enumerate(EXP_UNITS) for x, k, at in unit}

        def run_tiles(eng, m, stages):
            def turn(t, par):
                for k, f in enumerate(stages):
                    if f is None:
                        continue
                    if isinstance(t, int):
                        if 0 <= t - k < ETILES:
                            f(t - k, (t - k) % 2, ETILES * m + t - k)
                    else:
                        f(t - k if k else t, (par - k) % 2, t + (ETILES * m - k))
            first = 4
            last = first + (ETILES - first) // 2 * 2
            for t in range(first):
                turn(t, None)
            with eng.Fori(first, last, 2) as t:
                turn(t, 0)
                turn(t + 1, 1)
            for t in range(last, ETILES + 2):
                turn(t, None)

        def second_weights(i):
            bank = ps[:, 4 + i % 2, :]
            heads4 = bank.rearrange("p (h d) -> p h d", h=4 * P // DH)
            hs = 8 * (i % 2)
            if i < 4:
                h_, l_ = ((WQh, WQl), (WKh, WKl))[i // 2]
                return [(h_[:, hs:hs + 8], l_[:, hs:hs + 8], twice(heads4))]
            if i < 6:
                c = CH * (i - 4)
                return [(WVh[:, c:c + CH], WVl[:, c:c + CH], bank)]
            c = 4 * (i - 6)
            b4 = bank.rearrange("p (c n) -> p c n", c=4)
            return [(WOh[:, c:c + 4], WOl[:, c:c + 4], b4)]

        block = ctx.enter_context(nc.Block())

        @block.sync
        def _(sp):
            sp.dma_start(X[:], tokens.rearrange("b (t p) d -> p (b t) d", p=P)).then_inc(s_x_in, 16)
            sp.dma_start(XN[:, 0:FB, :], ins["L0_ffn_W1"].rearrange("(c p) d -> p c d", p=P)).then_inc(s_f_in, 16)
            sp.dma_start(XN[:, FB:2 * FB, :], ins["L0_ffn_W2"].rearrange("p (c f) -> p c f", c=FB)).then_inc(s_f_in, 16)
            cols = ((b1c[:], ins["L0_ffn_b1"].rearrange("(c p) -> p c", p=P)),
                    (normw[:], ins["L0_attn_norm_w"].rearrange("(p a) -> p a", a=1)),
                    (gamma[:], ins["L1_attn_ln_gamma"].rearrange("(p a) -> p a", a=1)),
                    (beta[:], ins["L1_attn_ln_beta"].rearrange("(p a) -> p a", a=1)),
                    (b2h[:], ins["L0_ffn_b2"].partition_broadcast(P)),
                    (bout[:], ins["L1_attn_b_out"].partition_broadcast(P)),
                    (bgate[:], ins["L1_ffn_bg"].partition_broadcast(P)))
            for dst, src in cols:
                sp.dma_start(dst, src, allow_slow_non_contiguous=True).then_inc(s_small_in, 16)
            for i in range(NPIECE):
                if i >= 2:
                    sp.wait_ge(s_w_lo, i - 1)
                sp.dma_start(stage_as(i), pieces[i][0]).then_inc(s_w_in[i % 2], 16)
            for ph, n in plan:
                if ph == "attn1":
                    sp.wait_ge(s_w_lo, NPIECE)
                    for i in range(2):
                        half = stage[:, i, :].rearrange("p (c d) -> p c d", d=D)
                        sp.dma_start(half, wqkv1[:, 8 * i:8 * i + 16, :]).then_inc(s_w_in[i], 16)
                    sp.wait_ge(s_w_tp, 4)
                    sp.dma_start(stage[:, 0, 0:INNER], wout1).then_inc(s_w_in[0], 16)
                if ph == "moe":
                    m = n["moe"]
                    sp.wait_ge(s_xs_sent, 16 * TOPK * NT * (m + 1))
                    sp.wait_ge(s_zero_in, 16)
                    sp.dma_start(XSt, x_sorted.rearrange("(t p) d -> p t d", p=P)).then_inc(s_xs_in, 16)
                    base = ETILES * m
                    with sp.Fori(0, ETILES // 2) as i:
                        for k in range(2):
                            sp.wait_ge(s_y_sb, i * 2 + (base + k + 1))
                            sp.dma_start(y_sorted[ds(i * (2 * P) + k * P, P), :], YS[:, k, :]).then_inc(s_y_out[k], 16)
                    for t in range(ETILES // 2 * 2, ETILES):
                        sp.wait_ge(s_y_sb, base + t + 1)
                        sp.dma_start(y_sorted[t * P:(t + 1) * P, :], YS[:, t % 2, :]).then_inc(s_y_out[t % 2], 16)
            sp.wait_ge(s_x_done, len(plan))
            sp.dma_start(out.rearrange("b (t p) d -> p (b t) d", p=P), X[:]).then_inc(s_out_done, 16)
            sp.wait_ge(s_out_done, 16)

        @block.gpsimd
        def _(pool):
            g = nc.gpsimd
            step = stepper(pool, s_pool_step)
            g.memset(ones32[:], 1.0)
            g.memset(onesh[:], 1.0)
            g.memset(neghalf[:], -0.5)
            g.memset(mask_qk[:], 0.0)
            step(g.memset(mask_kq[:], 0.0))
            g.affine_select(out=ident[:], in_=ones32[:], pattern=[[-1, P]], compare_op=ALU.is_equal, fill=0.0,
                            base=0, channel_multiplier=1)
            g.affine_select(out=before[:], in_=onesh[:], pattern=[[1, P]], compare_op=ALU.is_gt, fill=0.0,
                            base=0, channel_multiplier=-1)
            g.affine_select(out=mask_qk[:], in_=mask_qk[:], pattern=[[-1, P]], compare_op=ALU.is_ge, fill=NEG,
                            base=0, channel_multiplier=1)
            step(g.affine_select(out=mask_kq[:], in_=mask_kq[:], pattern=[[1, P]], compare_op=ALU.is_ge, fill=NEG,
                                 base=0, channel_multiplier=-1))
            g.tensor_copy(identh[:], ident[:])
            g.iota(iota_e[:], pattern=[[0, NT], [1, EXPERTS]], base=0, channel_multiplier=0,
                   allow_small_or_imprecise_dtypes=True)
            g.iota(iota_t[:], pattern=[[1, ETILES], [0, EXPERTS]], base=0, channel_multiplier=0,
                   allow_small_or_imprecise_dtypes=True)
            step(g.memset(upto[:], 1.0))
            g.affine_select(out=upto[:], in_=upto[:], pattern=[[1, EXPERTS], [-1, EXPERTS]], compare_op=ALU.is_ge,
                            fill=0.0, base=0, channel_multiplier=0)
            step(g.tensor_copy(identb[:], ident[:]))
            pool.wait_ge(s_small_in, 16 * 7)
            step(g.tensor_scalar(b2h[:], b2h[:], 0.5, None, ALU.mult))
            g.tensor_scalar(small[:, 4:5], b2h[:, 0:1], 0.0, None, ALU.mult).then_inc(s_const_pool, 1)
            if "moe" in phases:
                zeros = XTh[:, 0:2 * D]
                step(g.memset(zeros, 0.0))
                g.dma_start(x_sorted.rearrange("(t p) d -> p t d", p=P),
                            zeros.unsqueeze(1).broadcast_to([P, ETILES, 2 * D])).then_inc(s_zero_in, 16)
                pool.wait_ge(s_zero_in, 16)

            def norm(n, twice_normed):
                pool.wait_ge(s_ln_mv, n + 1)
                var = mv[:, :, 1]
                step(g.tensor_scalar(pw[:, 0, :], var, LN_EPS, None, ALU.add))
                if twice_normed is None:
                    g.tensor_tensor(rstd[:], pw[:, 0, :], neghalf[:], ALU.pow).then_inc(s_ln_rstd, 1)
                    return
                step(g.tensor_tensor(pw[:, 1, :], pw[:, 0, :], neghalf[:], ALU.pow))
                step(g.tensor_tensor(pw[:, 2, :], pw[:, 1, :], pw[:, 1, :], ALU.mult))
                step(g.tensor_tensor(pw[:, 3, :], pw[:, 2, :], var, ALU.mult))
                step(g.tensor_scalar(pw[:, 3, :], pw[:, 3, :], twice_normed, None, ALU.add))
                step(g.tensor_tensor(pw[:, 2, :], pw[:, 3, :], neghalf[:], ALU.pow))
                g.tensor_tensor(rstd[:], pw[:, 1, :], pw[:, 2, :], ALU.mult).then_inc(s_ln_rstd, 1)

            based = [0]

            def add_to_x(row, n):
                pool.wait_ge(s_ln_xn, NCH * (n + 1))
                g.tensor_tensor(X[:], X[:], row.unsqueeze(1).broadcast_to([P, NT, D]), ALU.add
                                ).then_inc(s_x_based, 1)
                based[0] += 1
                pool.wait_ge(s_x_based, based[0])

            def ffn(n, f):
                add_to_x(b2h[:], n)
                for u in range(NCH * FB):
                    c = u // FB
                    pool.wait_ge(s_h_relu, NCH * FB * f + u + 1)
                    if c >= 2:
                        pool.wait_ge(s_dn_ps, NCH * f + c - 1)
                    g.tensor_copy(HH[:, c % 2, u % FB, :], h32[:, u % 2, :]).then_inc(s_h_hi, 1)

            def attention(n, a, second):
                if second:
                    add_to_x(bout[:], n)
                pool.wait_ge(s_ln_lo, NCH * (n + 1))
                base = a * ITEMS
                g.memset(Q2[64:128], 0.0)
                step(g.memset(K2[64:128], 0.0))
                step(g.affine_select(out=K2[64:128], in_=K2[64:128],
                                     pattern=[[0, RING], [-1, 2], [0, CH]], compare_op=ALU.not_equal, fill=1.0,
                                     base=0, channel_multiplier=1))
                step(g.memset(VH, 1.0))
                g.tensor_scalar(small[:, 5:6], ones32[:, 0:1], 1.0, None, ALU.mult).then_inc(s_k2_set, 1)

                def body(t):
                    p, m, s, v, o = items(t)
                    for u in range(5):
                        if s is not None:
                            pool.wait_ge(s_ph, 5 * (base + s) + u + 1)
                            g.tensor_tensor(PL[:, s & 1, u, :], P32[:, u, :], PH[:, s & 1, u, :], ALU.subtract
                                            ).then_inc(s_pl, 1)
                    if v is not None:
                        pool.wait_ge(s_oh, base + v + 1)
                        g.tensor_tensor(OL.rearrange("p a b -> p (a b)"), O32.rearrange("p a b c -> p (a b c)"),
                                        OH.rearrange("p a b -> p (a b)"), ALU.subtract).then_inc(s_ol, 1)
                run_items(pool, body)

            def moe(n, m):
                for j in range(TOPK):
                    for t in range(NT):
                        if j == 0 and t == 0:
                            pool.wait_ge(s_r_pos, m + 1)
                            pool.wait_ge(s_zero_in, 16)
                        pool.wait_ge(s_xs_rdy, TOPK * NT * m + j * NT + t + 1)
                        g.indirect_dma_start(
                            x_sorted, bass.IndirectOffsetOnAxis(ap=posi[:, j, t:t + 1], axis=0),
                            XSs[:, t, j].rearrange("p a b -> p (a b)"), None).then_inc(s_xs_sent, 16)
                pool.wait_ge(s_y_out[0], 16 * stored(m + 1, 0))
                pool.wait_ge(s_y_out[1], 16 * stored(m + 1, 1))
                pool.wait_ge(s_xs_sent, 16 * TOPK * NT * (m + 1))
                for t in range(NT):
                    for j in range(TOPK):
                        g.indirect_dma_start(
                            Gy[:, (t * TOPK + j) * D:(t * TOPK + j + 1) * D], None, y_sorted,
                            bass.IndirectOffsetOnAxis(ap=posi[:, j, t:t + 1], axis=0)).then_inc(s_y_got[t // 4], 16)

            for ph, n in plan:
                norm(n["norm"], {"attn0": RMS_EPS, "attn1": LN_EPS}.get(ph))
                if ph == "ffn":
                    ffn(n["norm"], n["ffn"])
                elif ph == "moe":
                    moe(n["norm"], n["moe"])
                else:
                    attention(n["norm"], n["attn"], ph == "attn1")

        @block.scalar
        def _(act):
            a_ = nc.scalar
            for i, (src, cols, view, hi, lo) in enumerate(pieces):
                act.wait_ge(s_w_in[i % 2], 16 * (i // 2 + 1))
                a_.activation(hi, view(stage[:, i % 2, 0:cols]), ACT.Copy, scale=W_UP).then_inc(s_w_hi, 1)

            def norm(n, mode):
                for c in range(NCH):
                    act.wait_ge(s_ln_tp, NCH * n + c + 1)
                    o = XTh[:, c * CH:(c + 1) * CH]
                    if mode == "plain":
                        ins_ = a_.activation(o, ps[:, c % 2, :], ACT.Copy)
                    elif mode == "scaled":
                        ins_ = a_.activation(o, ps[:, c % 2, :], ACT.Copy, scale=normw[:])
                    else:
                        ins_ = a_.activation(o, ps[:, c % 2, :], ACT.Identity, scale=gamma[:], bias=beta[:])
                    ins_.then_inc(s_ln_hi, 1)

            def ffn(n, f):
                for u in range(NCH * FB):
                    act.wait_ge(s_up_ps, NCH * FB * f + u + 1)
                    if u >= 2:
                        act.wait_ge(s_h_lo, NCH * FB * f + u - 1)
                    a_.activation(h32[:, u % 2, :], ps[:, 2 + u % 2, :], ACT.Relu,
                                  bias=b1c[:, u % FB:u % FB + 1]).then_inc(s_h_relu, 1)

            def attention(n, a, second):
                base = a * ITEMS
                if second:
                    for i in range(8):
                        act.wait_ge(s_w_tp, i + 1)
                        for hi, lo, src in second_weights(i):
                            ins_ = a_.activation(hi, src, ACT.Copy, scale=W_UP)
                        ins_.then_inc(s_w_hi, 1)
                else:
                    act.wait_ge(s_g_ps, 1)
                    a_.activation(gates[:].rearrange("p a b -> p (a b)"), ps[:, 2, 0:NT * HEADS], ACT.Exp,
                                  scale=-1.0 / W_UP).then_inc(s_g_exp, 1)
                act.wait_ge(s_k2_set, a + 1)

                def body(t):
                    p, m, s, v, o = items(t)

                    def exps(u):
                        act.wait_ge(s_st_ps, 5 * (base + s) + u + 1)
                        if later(s, 1):
                            act.wait_ge(s_pl, 5 * (base + s) - 5 + u + 1)
                        a_.activation(P32[:, u, :], ps[:, 4 + u % 2, :], ACT.Exp).then_inc(s_ex_p, 1)

                    def hi(i):
                        x, isk = i // 2, i % 2
                        bank = (0, 1, 1, 0)[i]
                        act.wait_ge(s_qk_ps, 4 * (base + p) + i + 1)
                        if i == 0 and later(p, RING):
                            act.wait_ge(s_st_ps, 5 * (base + p) - 5 * (RING - 1))
                        dst = (K1 if isk else Q1)[:, p & (RING - 1), x, :]
                        a_.activation(dst, ps[:, bank, :], ACT.Copy, scale=1.0 / W_UP if isk else Q_SCALE
                                      ).then_inc(s_qk_hi, 1)
                    for u in range(5):
                        if s is not None:
                            exps(u)
                        if p is not None and u in (0, 1, 3, 4):
                            hi((0, 1, None, 2, 3)[u])
                        if o is not None and u == 2:
                            act.wait_ge(s_oth_ps, base + o + 1)
                            if later(o, 1):
                                act.wait_ge(s_op_ps, base + o)
                            a_.activation(OTh, ps[:, 0, 0:CH // 2].bitcast(F16), ACT.Copy).then_inc(s_oth_sb, 1)
                        if o is not None and u == 4:
                            act.wait_ge(s_otl_ps, base + o + 1)
                            a_.activation(OTl, ps[:, 1, 0:CH // 2].bitcast(F16), ACT.Copy).then_inc(s_otl_sb, 1)
                    if p is not None:
                        act.wait_ge(s_v_ps, base + p + 1)
                        if later(p, RING):
                            act.wait_ge(s_av_ps, 2 * (base + p) - 2 * (RING - 1))
                        a_.activation(VH[:, p & (RING - 1), :, :, 0:DH],
                                      ps[:, 0, :].rearrange("p (a b c) -> p a b c", a=TPB, b=2), ACT.Copy,
                                      scale=1.0 / W_UP).then_inc(s_v_hi, 1)
                    if m is not None:
                        act.wait_ge(s_mt_ps, base + m + 1)
                        for x in range(2):
                            a_.activation(Q2[64:66, m & (RING - 1), x, :], ps[0:2, 3, :], ACT.Copy, scale=-1.0,
                                          bias=EXP_LIFT).then_inc(s_mt_sb, 1)
                run_items(act, body)

            def moe(n, m):
                act.wait_ge(s_r_exp, 2 * m + 1)
                a_.activation(wts[:, 1, :], wts[:, 0, :], ACT.Exp).then_inc(s_r_exp, 1)

                def transposed(t, k, w):
                    act.wait_ge(s_t_ps, w + 1)
                    if not isinstance(t, int) or t >= 2:
                        act.wait_ge(s_ab_ps, w - 1)
                    a_.activation(XTt[:, k], ps[:, 0, 0:2 * P].rearrange("p (a b) -> p a b", a=2), ACT.Copy
                                  ).then_inc(s_t_sb, 1)

                def gate(t, k, w):
                    act.wait_ge(s_ab_ps, w + 1)
                    if not isinstance(t, int) or t >= 2:
                        act.wait_ge(s_g32_rdy, w - 1)
                    a_.activation(SA[:, k, :], ps[:, 1 + k, :], ACT.Silu, scale=1.0 / W_UP).then_inc(s_a_sb, 1)
                run_tiles(act, m, (transposed, gate, None))

            for ph, n in plan:
                norm(n["norm"], {"attn0": "scaled", "attn1": "affine"}.get(ph, "plain"))
                if ph == "ffn":
                    ffn(n["norm"], n["ffn"])
                elif ph == "moe":
                    moe(n["norm"], n["moe"])
                else:
                    attention(n["norm"], n["attn"], ph == "attn1")

        @block.vector
        def _(dve):
            v_ = nc.vector
            step = stepper(dve, s_dve_step)

            if "ffn" in phases:
                dve.wait_ge(s_f_in, 32)
                for k in range(2):
                    v_.tensor_reduce(fsm[:, k, 0:1], XN[:, FB * k:FB * (k + 1), :], AX.XY, ALU.add,
                                     apply_absolute_value=True).then_inc(s_f_abs, 1)
                dve.wait_ge(s_f_sum, 1)
                for k in range(2):
                    step(v_.tensor_scalar(fsm[:, k, 1:2], ps[:, 0, k:k + 1], 1.0 / (DFF * D), 1e-5, ALU.mult, ALU.add))
                    step(v_.tensor_scalar(fsm[:, k, 2:3], fsm[:, k, 1:2], 0.5, None, ALU.mult))
                    step(v_.tensor_scalar(fsm[:, k, 3:4], fsm[:, k, 1:2], -0.5, None, ALU.mult))
                    w = XN[:, FB * k:FB * (k + 1), :]
                    low = XN[:, 2 * FB + FB * k:2 * FB + FB * (k + 1), :]
                    step(v_.tensor_scalar(low, w, fsm[:, k, 3:4], None, ALU.is_lt))
                    v_.scalar_tensor_tensor(w, w, fsm[:, k, 2:3], low, ALU.is_gt, ALU.subtract
                                            ).then_inc(s_f_tern, 1)
                for k, dst in enumerate((F1, F2)):
                    dve.wait_ge(s_f_tp, k + 1)
                    v_.tensor_copy(dst[:].rearrange("p a b -> p (a b)"), ps[:, 1 + k, :]).then_inc(s_f_got, 1)
            def low_parts(lo, src, hi):
                if len(lo.shape) == 4 and lo.shape[2] == 2:
                    for k in range(2):
                        ins_ = v_.scalar_tensor_tensor(lo[:, :, k], src[:, :, k], W_UP, hi[:, :, k], ALU.mult,
                                                       ALU.subtract)
                    return ins_
                return v_.scalar_tensor_tensor(lo, src, W_UP, hi, ALU.mult, ALU.subtract)

            for i, (src, cols, view, hi, lo) in enumerate(pieces):
                dve.wait_ge(s_w_hi, i + 1)
                low_parts(lo, view(stage[:, i % 2, 0:cols]), hi).then_inc(s_w_lo, 1)

            def norm(n, mode):
                if n == 0:
                    dve.wait_ge(s_x_in, 16)
                if n >= 1:
                    dve.wait_ge(s_x_done, n)
                for t in range(NT):
                    ins_ = v_.bn_stats(bst[:, t, :], X[:, t, :])
                step(ins_)
                for t in range(NT):
                    ins_ = v_.bn_aggr(mv[:, t, :], bst[:, t, :])
                ins_.then_inc(s_ln_mv, 1)
                dve.wait_ge(s_ln_rstd, n + 1)
                for t in range(NT):
                    ins_ = v_.tensor_scalar(XN[:, t, :], X[:, t, :], mv[:, t, 0:1], rstd[:, t:t + 1],
                                            ALU.subtract, ALU.mult)
                    if t % TPC == TPC - 1:
                        ins_.then_inc(s_ln_xn, 1)
                for c in range(NCH):
                    dve.wait_ge(s_ln_hi, NCH * n + c + 1)
                    h = XTh[:, c * CH:(c + 1) * CH]
                    l = XTl[:, c * CH:(c + 1) * CH]
                    src = ps[:, c % 2, :]
                    if mode == "plain":
                        ins_ = v_.tensor_tensor(l, src, h, ALU.subtract)
                    elif mode == "scaled":
                        ins_ = v_.scalar_tensor_tensor(l, src, normw[:], h, ALU.mult, ALU.subtract)
                    else:
                        if c:
                            dve.wait_ge(s_ln_lo, NCH * n + c)
                        step(v_.tensor_scalar(T32[:], src, gamma[:], beta[:], ALU.mult, ALU.add))
                        ins_ = v_.tensor_tensor(l, T32[:], h, ALU.subtract)
                    ins_.then_inc(s_ln_lo, 1)

            def ffn(n, f, np_):
                def x_add(c):
                    dve.wait_ge(s_dn_ps, NCH * f + c + 1)
                    xs = X[:, TPC * c:TPC * (c + 1), :]
                    ins_ = v_.scalar_tensor_tensor(xs, ps[:, 4 + c % 2, :].rearrange("p (t d) -> p t d", t=TPC), 0.5,
                                                   xs, ALU.mult, ALU.add)
                    ins_.then_inc(s_x_att, 1)
                dve.wait_ge(s_x_based, np_)
                for u in range(NCH * FB):
                    c = u // FB
                    dve.wait_ge(s_h_hi, NCH * FB * f + u + 1)
                    v_.tensor_tensor(HL[:, c % 2, u % FB, :], h32[:, u % 2, :], HH[:, c % 2, u % FB, :], ALU.subtract
                                     ).then_inc(s_h_lo, 1)
                    if u % FB == 1 and c >= 1:
                        x_add(c - 1)
                x_add(NCH - 1)

            def attention(n, a, second, xa, np_, fb):
                base = a * ITEMS
                if second:
                    dve.wait_ge(s_x_based, np_)
                    for i in range(8):
                        dve.wait_ge(s_w_hi, NPIECE + i + 1)
                        for hi, lo, src in second_weights(i):
                            ins_ = low_parts(lo, src, hi)
                        ins_.then_inc(s_w_lo, 1)
                else:
                    dve.wait_ge(s_g_exp, 1)
                    step(v_.tensor_scalar(gates[:], gates[:], 1.0, None, ALU.add))
                    step(v_.reciprocal(gates[:], gates[:]))
                dve.wait_ge(s_k2_set, a + 1)

                def body(t):
                    p, m, s, v, o = items(t)

                    def maxima(u):
                        dve.wait_ge(s_mx_ps, 5 * (base + m) + u + 1)
                        if u == 0 and later(m, 1):
                            dve.wait_ge(s_mt_ps, base + m)
                        if u == 4:
                            ins_ = v_.tensor_reduce(MX[:, :, 1], ps[:, 2, :].rearrange("p (a b) -> p a b", a=2),
                                                    AX.X, ALU.max)
                        else:
                            for x, i, at in MAX_UNITS[u]:
                                ins_ = v_.tensor_reduce(MX[:, x, i:i + 1], ps[:, 2 + u % 2, at:at + P * (i + 1)],
                                                        AX.X, ALU.max)
                        ins_.then_inc(s_mx_red, 1)

                    def low(i):
                        x, isk = i // 2, i % 2
                        bank = (0, 1, 1, 0)[i]
                        r = p & (RING - 1)
                        dve.wait_ge(s_qk_hi, 4 * (base + p) + i + 1)
                        if isk:
                            dst = hi = K1[64:128, r, x, :]
                            src, c = ps[64:128, bank, :], 1.0 / W_UP
                        else:
                            dst, hi = Q2[0:64, r, x, :], Q1[0:64, r, x, :]
                            src, c = ps[0:64, bank, :], Q_SCALE
                        v_.scalar_tensor_tensor(dst, src, c, hi, ALU.mult, ALU.subtract).then_inc(s_qk_lo, 1)
                        if isk:
                            v_.tensor_copy(K2[0:64, r, x, :], K1[0:64, r, x, :]).then_inc(s_k2_cp, 1)

                    def p_high(u):
                        dve.wait_ge(s_ex_p, 5 * (base + s) + u + 1)
                        if u == 0 and later(s, 2):
                            dve.wait_ge(s_av_ps, 2 * (base + s) - 2)
                        v_.tensor_copy(PH[:, s & 1, u, :], P32[:, u, :]).then_inc(s_ph, 1)

                    def evacuate(x):
                        dve.wait_ge(s_av_ps, 2 * (base + v) + x + 1)
                        if x == 0 and later(v, 1):
                            dve.wait_ge(s_ol, base + v)
                        o4 = ps[:, 6 + x, 0:TPB * (DH + 1)].rearrange("p (a b) -> p a b", a=TPB)
                        nf = 2 if second else 4
                        v_.reciprocal(osc[:, x, 0, :], o4[:, :, DH]).then_inc(s_o_f, 1)
                        dve.wait_ge(s_o_f, fb + nf * v + (x + 1 if second else 2 * x + 1))
                        fac = osc[:, x, 0, :]
                        if not second:
                            gt = gates[:, ds(seq_of(v) * TPB, TPB), ds((v & (PAIRS - 1)) * 2 + x, 1)]
                            v_.tensor_tensor(osc[:, x, 1, :].unsqueeze(2), osc[:, x, 0, :].unsqueeze(2), gt, ALU.mult
                                             ).then_inc(s_o_f, 1)
                            dve.wait_ge(s_o_f, fb + nf * v + 2 * x + 2)
                            fac = osc[:, x, 1, :]
                        v_.tensor_tensor(O32[:, :, x, :], o4[:, :, 0:DH], fac.unsqueeze(2).broadcast_to([P, TPB, DH]),
                                         ALU.mult).then_inc(s_o_ev, 1)
                    for u in range(5):
                        if m is not None:
                            maxima(u)
                        if p is not None and u in (0, 1, 3, 4):
                            low((0, 1, None, 2, 3)[u])
                        if s is not None:
                            p_high(u)
                        if u == 2 and v is not None:
                            evacuate(0)
                    if p is not None:
                        r = p & (RING - 1)
                        dve.wait_ge(s_v_hi, base + p + 1)
                        v_.scalar_tensor_tensor(VL[:, r].rearrange("p a b c -> p (a b) c"),
                                                ps[:, 0, :].rearrange("p (a c) -> p a c", a=2 * TPB), 1.0 / W_UP,
                                                VH[:, r].rearrange("p a b c -> p (a b) c")[:, :, 0:DH],
                                                ALU.mult, ALU.subtract
                                                ).then_inc(s_v_lo, 1)
                    if v is not None:
                        evacuate(1)
                        dve.wait_ge(s_o_ev, 2 * (base + v) + 2)
                        if later(v, 1):
                            dve.wait_ge(s_oth_ps, base + v)
                        v_.tensor_copy(OH.rearrange("p a b -> p (a b)"), O32.rearrange("p a b c -> p (a b c)")
                                       ).then_inc(s_oh, 1)
                    if o is not None:
                        dve.wait_ge(s_op_ps, base + o + 1)
                        dve.wait_ge(s_x_att, xa + o)
                        xs = X[:, ds(seq_of(o) * TPB, TPB), :]
                        v_.scalar_tensor_tensor(xs, ps[:, 1, :].rearrange("p (t d) -> p t d", t=TPB), 1.0 / W_UP, xs,
                                                ALU.mult, ALU.add).then_inc(s_x_att, 1)
                run_items(dve, body)

            def moe(n, m):
                dve.wait_ge(s_r_ps, m + 1)
                step(v_.tensor_scalar(logits, ps[:, 2, 0:NT * EXPERTS].rearrange("p (t e) -> p t e", t=NT), 1.0 / W_UP,
                                      None, ALU.mult))
                step(v_.tensor_tensor(logits, logits, bgate[:].unsqueeze(1).broadcast_to([P, NT, EXPERTS]), ALU.add))
                for t in range(NT):
                    ins_ = v_.max(top8[:, t, :], logits[:, t, :])
                step(ins_)
                for t in range(NT):
                    ins_ = v_.max_index(idx8[:, t, :], top8[:, t, :], logits[:, t, :])
                step(ins_)
                v_.tensor_tensor(wts[:, 0, :], top8[:, :, 1], top8[:, :, 0], ALU.subtract).then_inc(s_r_exp, 1)
                for j in range(TOPK):
                    ins_ = v_.tensor_copy(idxf[:, j, :], idx8[:, :, j])
                step(ins_)
                for j in range(TOPK):
                    ins_ = v_.tensor_tensor(hot[:, j], iota_e[:], idxf[:, j, :].unsqueeze(2).broadcast_to([P, NT, EXPERTS]),
                                            ALU.is_equal)
                step(ins_)
                v_.tensor_tensor(hoth, hot[:, 0], hot[:, 1], ALU.add).then_inc(s_r_hot, 1)
                dve.wait_ge(s_r_exp, 2 * m + 2)
                step(v_.tensor_scalar(wts[:, 0, :], wts[:, 1, :], 1.0, None, ALU.add))
                step(v_.reciprocal(wts[:, 2, :], wts[:, 0, :]))
                step(v_.tensor_tensor(wts[:, 3, :], wts[:, 1, :], wts[:, 2, :], ALU.mult))
                dve.wait_ge(s_r_rank, m + 1)
                step(v_.tensor_scalar(cnt[:, 0, :], ps[:, 4, 0:EXPERTS], float(P - 1), None, ALU.add))
                step(v_.tensor_copy(cnt_i[:, 0, :], cnt[:, 0, :]))
                step(v_.tensor_scalar(cnt_i[:, 1, :], cnt_i[:, 0, :], int(math.log2(P)), None, ALU.logical_shift_right))
                step(v_.tensor_copy(cnt[:, 1, :], cnt_i[:, 1, :]))
                step(v_.tensor_tensor(cum, upto[:], cnt[:, 1, :].unsqueeze(1).broadcast_to([P, EXPERTS, EXPERTS]),
                                      ALU.mult))
                step(v_.tensor_reduce(cnt[:, 2, :], cum, AX.X, ALU.add))
                step(v_.tensor_tensor(cnt[:, 3, :], cnt[:, 2, :], cnt[:, 1, :], ALU.subtract))
                step(v_.tensor_scalar(cnt[:, 3, :], cnt[:, 3, :], float(P), None, ALU.mult))
                step(v_.tensor_tensor(prod[:, 0], ps[:, 3, 0:NT * EXPERTS].rearrange("p (t e) -> p t e", t=NT),
                                      cnt[:, 3, :].unsqueeze(1).broadcast_to([P, NT, EXPERTS]), ALU.add))
                step(v_.tensor_tensor(prod[:, 1], prod[:, 0], hot[:, 1], ALU.mult))
                step(v_.tensor_tensor(prod[:, 0], prod[:, 0], hot[:, 0], ALU.mult))
                step(v_.tensor_reduce(posf, prod, AX.X, ALU.add))
                v_.tensor_copy(posi, posf).then_inc(s_r_pos, 1)
                step(v_.tensor_tensor(tile_e8, iota_t[:], cnt[:, 2, :].unsqueeze(1).broadcast_to([P, ETILES, EXPERTS]),
                                      ALU.is_ge))
                step(v_.tensor_reduce(tile_e[:, 0, 0:ETILES], tile_e8, AX.X, ALU.add))
                step(v_.tensor_scalar(tile_e[:, 1, 0:ETILES], tile_e[:, 0, 0:ETILES], float(EXPERTS - 1), None, ALU.min))
                step(v_.tensor_copy(tile_ei[:, 0:ETILES], tile_e[:, 1, 0:ETILES]))
                v_.tensor_copy(small[:, 0:1], tile_e[:, 1, 0:1]).then_inc(s_r_hot, 1)
                for j in range(TOPK):
                    for t in range(NT):
                        buf = T32[:, (t % 4) * D:(t % 4 + 1) * D]
                        step(v_.tensor_scalar(buf, XN[:, t, :], wts[:, 2 + j, t:t + 1], None, ALU.mult))
                        step(v_.tensor_copy(XSs[:, t, j, 0, :], buf))
                        v_.tensor_tensor(XSs[:, t, j, 1, :], buf, XSs[:, t, j, 0, :], ALU.subtract
                                         ).then_inc(s_xs_rdy, 1)

                def product(t, k, w):
                    dve.wait_ge(s_a_sb, w + 1)
                    if not isinstance(t, int) or t >= 2:
                        dve.wait_ge(s_g_lo, w - 1)
                    v_.scalar_tensor_tensor(G32[:, k, :], ps[:, 3 + k, :], 1.0 / W_UP, SA[:, k, :], ALU.mult, ALU.mult
                                            ).then_inc(s_g32_rdy, 1)
                    dve.wait_ge(s_g32_rdy, w + 1)
                    if not isinstance(t, int) or t >= 2:
                        dve.wait_ge(s_y_ps, w - 1)
                    gh = GH[:, k].rearrange("p a b -> p (a b)")
                    v_.tensor_copy(gh, G32[:, k, :]).then_inc(s_g_hi, 1)
                    dve.wait_ge(s_g_hi, w + 1)
                    v_.tensor_tensor(GL[:, k].rearrange("p a b -> p (a b)"), G32[:, k, :], gh, ALU.subtract
                                     ).then_inc(s_g_lo, 1)

                def result(t, k, w):
                    dve.wait_ge(s_y_ps, w + 1)
                    if not isinstance(t, int) or t >= 2:
                        dve.wait_ge(s_y_out[k], (t >> 1) * 16 + 16 * stored(m, k))
                    v_.tensor_scalar(YS[:, k, :], ps[:, 5 + k, 0:D], 0.5 / W_UP, None, ALU.mult).then_inc(s_y_sb, 1)
                run_tiles(dve, m, (None, product, result))
                dve.wait_ge(s_xs_sent, 16 * TOPK * NT * (m + 1))
                for t in range(NT):
                    x1 = X[:, t, :]
                    step(v_.scalar_tensor_tensor(x1, XN[:, t, :], 0.5, x1, ALU.mult, ALU.add))
                for t in range(NT):
                    for j in range(TOPK):
                        if j == 0 and t % 4 == 0:
                            dve.wait_ge(s_y_got[t // 4], 16 * TOPK * 4 * (m + 1))
                        at = (t * TOPK + j) * D
                        step(v_.tensor_tensor(X[:, t, :], X[:, t, :], Gy[:, at:at + D], ALU.add))

            xa = np_ = fb = 0
            for i, (ph, n) in enumerate(plan):
                norm(n["norm"], {"attn0": "scaled", "attn1": "affine"}.get(ph, "plain"))
                if ph == "ffn":
                    np_ += 1
                    ffn(n["norm"], n["ffn"], np_)
                    xa += NCH
                elif ph == "moe":
                    moe(n["norm"], n["moe"])
                else:
                    np_ += ph == "attn1"
                    attention(n["norm"], n["attn"], ph == "attn1", xa, np_, fb)
                    fb += (2 if ph == "attn1" else 4) * ITEMS
                    xa += ITEMS
                dve.wait_ge(s_x_att, xa)
                v_.tensor_copy(small[:, 1:2], X[:, NT - 1, D - 1:D]).then_inc(s_x_done, 1)

        @block.tensor
        def _(pe):
            mm = nc.tensor.matmul
            pe.wait_ge(s_const_pool, 1)
            if "ffn" in phases:
                pe.wait_ge(s_f_abs, 2)
                for k in range(2):
                    ins_ = mm(ps[:, 0, k:k + 1], ones32[:], fsm[:, k, 0:1], start=True, stop=True)
                ins_.then_inc(s_f_sum, 1)
                for k in range(2):
                    pe.wait_ge(s_f_tern, k + 1)
                    for c in range(FB):
                        ins_ = nc.tensor.transpose(ps[:, 1 + k, c * P:(c + 1) * P], XN[:, FB * k + c, :], ident[:])
                    ins_.then_inc(s_f_tp, 1)
                pe.wait_ge(s_f_got, 2)

            def norm(n):
                for c in range(NCH):
                    pe.wait_ge(s_ln_xn, NCH * n + c + 1)
                    if c >= 2:
                        pe.wait_ge(s_ln_lo, NCH * n + c - 1)
                    for i in range(TPC):
                        ins_ = nc.tensor.transpose(ps[:, c % 2, i * P:(i + 1) * P], XN[:, TPC * c + i, :], ident[:])
                    ins_.then_inc(s_ln_tp, 1)

            def split_mm(dst, sh, sl, mh, ml, inc=None):
                mm(dst, sh, mh, start=True, stop=False)
                mm(dst, sh, ml, start=False, stop=False)
                ins_ = mm(dst, sl, mh, start=False, stop=True)
                if inc is not None:
                    ins_.then_inc(inc, 1)
                return ins_

            def ffn(n, f):
                def down(c):
                    pe.wait_ge(s_h_lo, NCH * FB * f + FB * (c + 1))
                    for i in range(TPC):
                        for k in range(FB):
                            for part in (HH, HL):
                                ins_ = mm(ps[:, 4 + c % 2, i * D:(i + 1) * D], part[:, c % 2, k, i * P:(i + 1) * P],
                                          F2[:, k, :], start=(k == 0 and part is HH), stop=(k == FB - 1 and part is HL))
                    ins_.then_inc(s_dn_ps, 1)
                for c in range(NCH):
                    pe.wait_ge(s_ln_lo, NCH * n + c + 1)
                    for k in range(FB):
                        u = FB * c + k
                        if u >= 2:
                            pe.wait_ge(s_h_relu, NCH * FB * f + u - 1)
                        mm(ps[:, 2 + u % 2, :], F1[:, k, :], XTh[:, c * CH:(c + 1) * CH], start=True, stop=False)
                        mm(ps[:, 2 + u % 2, :], F1[:, k, :], XTl[:, c * CH:(c + 1) * CH], start=False, stop=True
                           ).then_inc(s_up_ps, 1)
                    if c >= 1:
                        down(c - 1)
                down(NCH - 1)

            def attention(n, a, second, xa):
                base = a * ITEMS
                pe.wait_ge(s_ln_lo, NCH * (n + 1))
                if second:
                    for i in range(8):
                        if i >= 2:
                            pe.wait_ge(s_w_lo, NPIECE + i - 1)
                        if i == 0:
                            pe.wait_ge(s_w_in[0], 16 * ((NPIECE + 1) // 2 + 1))
                            pe.wait_ge(s_w_in[1], 16 * (NPIECE // 2 + 1))
                        if i == 6:
                            pe.wait_ge(s_w_in[0], 16 * ((NPIECE + 1) // 2 + 2))
                        for b in range(4):
                            c = 4 * i + b
                            if c < 16:
                                src = stage[:, 0, c * D:(c + 1) * D]
                            elif c < 24:
                                src = stage[:, 1, (c - 8) * D:(c - 7) * D]
                            else:
                                src = stage[:, 0, (c - 24) * P:(c - 23) * P]
                            ins_ = nc.tensor.transpose(ps[:, 4 + i % 2, b * P:(b + 1) * P], src, ident[:])
                        ins_.then_inc(s_w_tp, 1)
                    pe.wait_ge(s_w_lo, NPIECE + 8)
                else:
                    pe.wait_ge(s_w_lo, NPIECE)
                    for t in range(NT):
                        tok = slice(t * P, (t + 1) * P)
                        split_mm(ps[:, 2, t * HEADS:(t + 1) * HEADS], XTh[:, tok], XTl[:, tok], WGh[:], WGl[:],
                                 s_g_ps if t == NT - 1 else None)
                    pe.wait_ge(s_g_exp, 1)

                def body(t):
                    p, m, s, v, o = items(t)

                    def project(i):
                        x, isk = i // 2, i % 2
                        bank = (0, 1, 1, 0)[i]
                        if i == 0:
                            if later(p, 1):
                                pe.wait_ge(s_v_lo, base + p)
                        elif i == 1:
                            if o is not None and later(o, 1):
                                pe.wait_ge(s_x_att, xa + o)
                            elif later(p, 1):
                                pe.wait_ge(s_qk_lo, 4 * (base + p) - 1)
                        elif i == 2:
                            pe.wait_ge(s_qk_lo, 4 * (base + p) + 2)
                        elif o is not None:
                            pe.wait_ge(s_oth_sb, base + o + 1)
                        else:
                            pe.wait_ge(s_qk_lo, 4 * (base + p) + 1)
                        wh, wl = (WKh, WKl) if isk else (WQh, WQl)
                        head = (p & (PAIRS - 1)) * 2 + x
                        seq = ds(seq_of(p) * SEQ, SEQ)
                        whf = wh[:].rearrange("p h a d -> p (h a d)")
                        wlf = wl[:].rearrange("p h a d -> p (h a d)")
                        split_mm(ps[:, bank, :], whf[:, ds(head * P, P)], wlf[:, ds(head * P, P)],
                                 XTh[:, seq], XTl[:, seq], s_qk_ps)

                    def project_v():
                        pe.wait_ge(s_qk_lo, 4 * (base + p) + 4)
                        for i in range(TPB):
                            tok = ds(seq_of(p) * SEQ + i * P, P)
                            hp = ds((p & (PAIRS - 1)) * P, P)
                            split_mm(ps[:, 0, i * P:(i + 1) * P], XTh[:, tok], XTl[:, tok], WVh[:, hp], WVl[:, hp],
                                     s_v_ps if i == TPB - 1 else None)

                    def maxima(u):
                        r = m & (RING - 1)
                        if u == 0:
                            pe.wait_ge(s_qk_lo, 4 * (base + m) + 2)
                        if u == 2:
                            pe.wait_ge(s_qk_lo, 4 * (base + m) + 4)
                        if u == 1:
                            if later(m, 1):
                                pe.wait_ge(s_mt_sb, 2 * (base + m))
                        else:
                            if u or later(m, 1):
                                pe.wait_ge(s_mx_red, 5 * (base + m) + (0, None, 1, 2, 3)[u])
                        for x, i, at in MAX_UNITS[u]:
                            mm(ps[:, 2 + u % 2, at:at + (i + 1) * P], Q1[:, r, x, i * P:(i + 1) * P],
                               K1[:, r, x, 0:(i + 1) * P], start=True, stop=False)
                            ins_ = mm(ps[:, 2 + u % 2, at + i * P:at + (i + 1) * P], identb[:], mask_qk[:],
                                      start=False, stop=True)
                        ins_.then_inc(s_mx_ps, 1)

                    def max_rows():
                        pe.wait_ge(s_mx_red, 5 * (base + m) + 5)
                        for i in range(TPB):
                            ins_ = nc.tensor.transpose(ps[0:2, 3, i * P:(i + 1) * P], MX[:, :, i], ident[:])
                        ins_.then_inc(s_mt_ps, 1)

                    def scores(u):
                        r = s & (RING - 1)
                        if u == 0:
                            pe.wait_ge(s_mt_sb, 2 * (base + s) + 2)
                            pe.wait_ge(s_k2_cp, 2 * (base + s) + 2)
                        if u >= 2 or later(s, 1):
                            pe.wait_ge(s_ex_p, 5 * (base + s) + (0, -1, 1, 2, 3)[u])
                        for x, k, at in EXP_UNITS[u]:
                            w = SEQ - k * P
                            blk = slice(k * P, (k + 1) * P)
                            dst = ps[:, 4 + u % 2, at:at + w]
                            mm(dst, K1[:, r, x, blk], Q1[:, r, x, k * P:SEQ], start=True, stop=False)
                            mm(dst, K2[:, r, x, blk], Q2[:, r, x, k * P:SEQ], start=False, stop=False)
                            ins_ = mm(ps[:, 4 + u % 2, at:at + P], identb[:], mask_kq[:], start=False, stop=True)
                        ins_.then_inc(s_st_ps, 1)

                    def outputs(x, blocks):
                        r, q2 = v & (RING - 1), v & 1
                        if blocks[0] == 0:
                            if x == 0:
                                pe.wait_ge(s_pl, 5 * (base + v) + 5)
                            if later(v, 1):
                                pe.wait_ge(s_o_ev, 2 * (base + v) - 1 + x)
                        for i in blocks:
                            c = i * (DH + 1)
                            for k in range(i + 1):
                                u, at = WHERE[x, k]
                                at += (i - k) * P
                                ph_, pl_ = PH[:, q2, u, at:at + P], PL[:, q2, u, at:at + P]
                                mm(ps[:, 6 + x, c:c + DH + 1], ph_, VH[:, r, k, x, 0:DH + 1], start=(k == 0), stop=False)
                                mm(ps[:, 6 + x, c:c + DH], ph_, VL[:, r, k, x, :], start=False, stop=False)
                                ins_ = mm(ps[:, 6 + x, c:c + DH + 1], pl_, VH[:, r, k, x, 0:DH + 1], start=False,
                                          stop=(k == i))
                        if blocks[-1] == TPB - 1:
                            ins_.then_inc(s_av_ps, 1)

                    def turn_outputs(part):
                        src, turned = ((OH, s_oth_ps), (OL, s_otl_ps))[part]
                        if part == 0:
                            pe.wait_ge(s_oh, base + o + 1)
                            if p is not None:
                                pe.wait_ge(s_qk_lo, 4 * (base + p) + 1)
                            else:
                                pe.wait_ge(s_v_lo, base + ITEMS)
                            if p is None and later(o, 1):
                                pe.wait_ge(s_oth_sb, base + o)
                        else:
                            pe.wait_ge(s_ol, base + o + 1)
                            if p is not None:
                                pe.wait_ge(s_qk_lo, 4 * (base + p) + 3)
                            else:
                                pe.wait_ge(s_x_att, xa + o)
                        for i in range(TPB):
                            ins_ = nc.tensor.transpose(ps[:, part, i * P // 2:(i + 1) * P // 2].bitcast(F16), src[:, i, :],
                                                       identh[:])
                        ins_.then_inc(turned, 1)

                    def project_out():
                        pe.wait_ge(s_oth_sb, base + o + 1)
                        pe.wait_ge(s_otl_sb, base + o + 1)
                        for i in range(TPB):
                            blk = slice(i * P, (i + 1) * P)
                            split_mm(ps[:, 1, i * D:(i + 1) * D], OTh[:, blk], OTl[:, blk],
                                     WOh[:].rearrange("p c n -> p (c n)")[:, ds((o & (PAIRS - 1)) * D, D)],
                                     WOl[:].rearrange("p c n -> p (c n)")[:, ds((o & (PAIRS - 1)) * D, D)],
                                     s_op_ps if i == TPB - 1 else None)

                    for u in range(5):
                        if p is not None and u in (0, 1, 3, 4):
                            project((0, 1, None, 2, 3)[u])
                        if m is not None:
                            maxima(u)
                        if s is not None:
                            scores(u)
                        if o is not None and u in (2, 4):
                            turn_outputs(u // 2 - 1)
                        if v is not None:
                            outputs(*((0, (0, 1)), (0, (2,)), (0, (3,)), (1, (0, 1, 2)), (1, (3,)))[u])
                    if p is not None:
                        project_v()
                    if m is not None:
                        max_rows()
                    if o is not None:
                        project_out()
                run_items(pe, body)

            def moe(n, m):
                pe.wait_ge(s_ln_lo, NCH * (n + 1))
                pe.wait_ge(s_w_lo, NPIECE)
                for t in range(NT):
                    tok = slice(t * P, (t + 1) * P)
                    split_mm(ps[:, 2, t * EXPERTS:(t + 1) * EXPERTS], XTh[:, tok], XTl[:, tok], RGh[:], RGl[:],
                             s_r_ps if t == NT - 1 else None)
                pe.wait_ge(s_r_hot, 2 * m + 1)
                mm(ps[:, 3, 0:NT * EXPERTS], before[:], hoth.rearrange("p t e -> p (t e)"), start=True, stop=False)
                for t in range(NT - 1):
                    mm(ps[:, 3, (t + 1) * EXPERTS:NT * EXPERTS].rearrange("p (t e) -> p t e", e=EXPERTS), onesh[:],
                       hoth[:, t, :].unsqueeze(1).broadcast_to([P, NT - 1 - t, EXPERTS]), start=False,
                       stop=(t == NT - 2))
                for t in range(NT):
                    ins_ = mm(ps[:, 4, 0:EXPERTS], onesh[:], hoth[:, t, :], start=(t == 0), stop=(t == NT - 1))
                ins_.then_inc(s_r_rank, 1)
                pe.wait_ge(s_r_hot, 2 * m + 2)
                pe.wait_ge(s_xs_in, 16 * (m + 1))

                def turned(t, k, w):
                    if not isinstance(t, int) or t >= 1:
                        pe.wait_ge(s_t_sb, w)
                    for part in range(2):
                        src = XSt.rearrange("p t d -> p (t d)")[:, ds(t * (2 * D) + part * D, D)]
                        ins_ = mm(ps[:, 0, part * P:(part + 1) * P], src, identh[:], start=True, stop=True)
                    ins_.then_inc(s_t_ps, 1)

                def expert(t):
                    return pe.value_load(tile_ei[0:1, ds(t, 1)], min_val=0, max_val=EXPERTS - 1)

                def up(t, k, w):
                    e = expert(t)
                    pe.wait_ge(s_t_sb, w + 1)
                    if not isinstance(t, int) or t >= 2:
                        pe.wait_ge(s_g32_rdy, w - 1)
                    for bank, wh, wl in ((1 + k, E1h, E1l), (3 + k, E3h, E3l)):
                        for f in range(HB):
                            whf = wh[:].rearrange("p e h -> p (e h)")[:, ds(e * H + f * P, P)]
                            wlf = wl[:].rearrange("p e h -> p (e h)")[:, ds(e * H + f * P, P)]
                            ins_ = split_mm(ps[:, bank, f * P:(f + 1) * P], whf, wlf, XTt[:, k, 0, :], XTt[:, k, 1, :])
                    ins_.then_inc(s_ab_ps, 1)

                def down(t, k, w):
                    e = expert(t)
                    pe.wait_ge(s_g_lo, w + 1)
                    if not isinstance(t, int) or t >= 2:
                        pe.wait_ge(s_y_sb, w - 1)
                    for f in range(HB):
                        wh = E2h[:].rearrange("p e c d -> p (e c d)")[:, ds(e * (HB * D) + f * D, D)]
                        wl = E2l[:].rearrange("p e c d -> p (e c d)")[:, ds(e * (HB * D) + f * D, D)]
                        dst = ps[:, 5 + k, 0:D]
                        mm(dst, GH[:, k, f, :], wh, start=(f == 0), stop=False)
                        mm(dst, GH[:, k, f, :], wl, start=False, stop=False)
                        ins_ = mm(dst, GL[:, k, f, :], wh, start=False, stop=(f == HB - 1))
                    ins_.then_inc(s_y_ps, 1)
                run_tiles(pe, m, (turned, up, down))

            xa = 0
            for ph, n in plan:
                norm(n["norm"])
                if ph == "ffn":
                    ffn(n["norm"], n["ffn"])
                    xa += NCH
                elif ph == "moe":
                    moe(n["norm"], n["moe"])
                else:
                    attention(n["norm"], n["attn"], ph == "attn1", xa)
                    xa += ITEMS


def kernel(**inputs):
    import numpy as _np
    import concourse.bacc as _bacc
    from concourse import mybir as _mybir
    from concourse.bass_utils import run_bass_kernel_spmd as _run

    nc = _bacc.Bacc("TRN2", target_bir_lowering=False, num_devices=1)
    arrays, args = {}, {}
    for name, a in inputs.items():
        a = _np.ascontiguousarray(a)
        arrays[f"in_{name}"] = a
        args[name] = nc.dram_tensor(f"in_{name}", a.shape, _mybir.dt.from_np(a.dtype), kind="ExternalInput").ap()
    shape = inputs["L0_attn_tokens"].shape
    out = nc.dram_tensor("out_x", shape, _mybir.dt.float32, kind="ExternalOutput").ap()
    macaron_block(nc, args, out, PHASES)
    return _run(nc, [arrays], core_ids=[0]).results[0]["out_x"]
```
